# Optimizing a Trainium2 kernel written in Bass

```python
import numpy as np
import jax
import jax.numpy as jnp

def _softmax(x, axis=-1):
    return jax.nn.softmax(x, axis=axis)

def _gelu(x):
    return jax.nn.gelu(x, approximate=True)

def _silu(x):
    return jax.nn.silu(x)

def _sigmoid(x):
    return jax.nn.sigmoid(x)

def _layernorm(x, axis=-1, eps=1e-05):
    m = jnp.mean(x, axis=axis, keepdims=True)
    v = jnp.var(x, axis=axis, keepdims=True)
    return (x - m) / jnp.sqrt(v + eps)

def _scatter_add(tgt, idx, src, axis=0):
    return tgt.at[idx].add(src)

def _segment_sum(src, seg, n):
    return jax.ops.segment_sum(src, seg, n)
kernel_name = 'mk_hybrid_d1_jaxref_r8_95f911'

def setup_inputs(seed: int=0):
    np.random.seed(seed)
    _w = jnp.asarray

    def _L0_attn_a_setup():
        import jax, jax.numpy as jnp
        import numpy as np
        import math
        D_MODEL, D_C, D_R, NH = (128, 128, 32, 16)
        HD = D_MODEL // NH
        B, T = (2, 256)

        def _rope_tables(T, d_R):
            inv_freq = 1.0 / 10000.0 ** (jnp.arange(0, d_R, 2, dtype=jnp.float32) / d_R)
            t = jnp.arange(T, dtype=jnp.float32)
            freqs = jnp.outer(t, inv_freq)
            return (jnp.cos(freqs), jnp.sin(freqs))

        def _rotary_apply(x, cos, sin):
            d = x.shape[-1]
            x1, x2 = (x[..., :d // 2], x[..., d // 2:])
            return jnp.concatenate([x1 * cos - x2 * sin, x2 * cos + x1 * sin], axis=-1)
        key = jax.random.key(seed)
        ks = jax.random.split(key, 8)
        s = lambda fan_in: 1.0 / math.sqrt(fan_in)
        return {'x': jax.random.normal(ks[0], (B, T, D_MODEL), jnp.float32), 'W_kv_down': jax.random.normal(ks[1], (D_MODEL, D_C), jnp.float32) * s(D_MODEL), 'W_k_up': jax.random.normal(ks[2], (D_C, D_MODEL), jnp.float32) * s(D_C), 'W_v_up': jax.random.normal(ks[3], (D_C, D_MODEL), jnp.float32) * s(D_C), 'W_q': jax.random.normal(ks[4], (D_MODEL, D_MODEL), jnp.float32) * s(D_MODEL), 'W_q_rope': jax.random.normal(ks[5], (D_MODEL, D_R), jnp.float32) * s(D_MODEL), 'W_k_rope': jax.random.normal(ks[6], (D_C, D_R), jnp.float32) * s(D_C), 'W_o': jax.random.normal(ks[7], (D_MODEL, D_MODEL), jnp.float32) * s(D_MODEL)}
    _L0_attn_a_in = _L0_attn_a_setup()

    def _L0_attn_b_setup():
        import jax, jax.numpy as jnp
        import numpy as np
        NUM_HEADS = 16
        USE_MASKING = True
        NEG_INF = -1000000000.0
        key = jax.random.key(seed)
        k1, k2 = jax.random.split(key)
        B, S, D = (2, 256, 128)
        x = jax.random.normal(k1, (B, S, D), dtype=jnp.float32)
        qkv_weights = jax.random.normal(k2, (D, 3 * D), dtype=jnp.float32) * (1.0 / np.sqrt(D))
        return {'x': x, 'qkv_weights': qkv_weights}
    _L0_attn_b_in = _L0_attn_b_setup()

    def _L0_ffn_setup():
        import jax, jax.numpy as jnp
        import numpy as np
        DIM = 128
        NUM_EXPERTS = 8
        HIDDEN = 512
        CAP_FACTOR = 2.0
        B, S = (4, 256)
        key = jax.random.key(seed)
        ks = jax.random.split(key, 6)
        scale_r = 1.0 / np.sqrt(DIM)
        scale_1 = 1.0 / np.sqrt(DIM)
        scale_2 = 1.0 / np.sqrt(HIDDEN)
        return {'x': jax.random.normal(ks[0], (B, S, DIM), dtype=jnp.float32), 'router_w': jax.random.uniform(ks[1], (NUM_EXPERTS, DIM), jnp.float32, -scale_r, scale_r), 'w1': jax.random.uniform(ks[2], (NUM_EXPERTS, DIM, HIDDEN), jnp.float32, -scale_1, scale_1), 'b1': jax.random.uniform(ks[3], (NUM_EXPERTS, HIDDEN), jnp.float32, -scale_1, scale_1), 'w2': jax.random.uniform(ks[4], (NUM_EXPERTS, HIDDEN, DIM), jnp.float32, -scale_2, scale_2), 'b2': jax.random.uniform(ks[5], (NUM_EXPERTS, DIM), jnp.float32, -scale_2, scale_2)}
    _L0_ffn_in = _L0_ffn_setup()
    _d = {'L0_attn_a_x': _L0_attn_a_in['x'], 'L0_attn_a_W_kv_down': _L0_attn_a_in['W_kv_down'], 'L0_attn_a_W_k_up': _L0_attn_a_in['W_k_up'], 'L0_attn_a_W_v_up': _L0_attn_a_in['W_v_up'], 'L0_attn_a_W_q': _L0_attn_a_in['W_q'], 'L0_attn_a_W_q_rope': _L0_attn_a_in['W_q_rope'], 'L0_attn_a_W_k_rope': _L0_attn_a_in['W_k_rope'], 'L0_attn_a_W_o': _L0_attn_a_in['W_o'], 'L0_attn_b_qkv_weights': _L0_attn_b_in['qkv_weights'], 'L0_ffn_router_w': _L0_ffn_in['router_w'], 'L0_ffn_w1': _L0_ffn_in['w1'], 'L0_ffn_b1': _L0_ffn_in['b1'], 'L0_ffn_w2': _L0_ffn_in['w2'], 'L0_ffn_b2': _L0_ffn_in['b2']}
    _x0 = _d['L0_attn_a_x']
    _d['L0_attn_a_x'] = jax.random.normal(jax.random.fold_in(jax.random.key(seed), 1), (2, 1024, 128), dtype=_x0.dtype)
    del _x0
    return _d

def reference(L0_attn_a_x, L0_attn_a_W_kv_down, L0_attn_a_W_k_up, L0_attn_a_W_v_up, L0_attn_a_W_q, L0_attn_a_W_q_rope, L0_attn_a_W_k_rope, L0_attn_a_W_o, L0_attn_b_qkv_weights, L0_ffn_router_w, L0_ffn_w1, L0_ffn_b1, L0_ffn_w2, L0_ffn_b2):

    def _L0_attn_a_ref(x, W_kv_down, W_k_up, W_v_up, W_q, W_q_rope, W_k_rope, W_o):
        import jax, jax.numpy as jnp
        import numpy as np
        import math
        D_MODEL, D_C, D_R, NH = (128, 128, 32, 16)
        HD = D_MODEL // NH
        B, T = (2, 256)

        def _rope_tables(T, d_R):
            inv_freq = 1.0 / 10000.0 ** (jnp.arange(0, d_R, 2, dtype=jnp.float32) / d_R)
            t = jnp.arange(T, dtype=jnp.float32)
            freqs = jnp.outer(t, inv_freq)
            return (jnp.cos(freqs), jnp.sin(freqs))

        def _rotary_apply(x, cos, sin):
            d = x.shape[-1]
            x1, x2 = (x[..., :d // 2], x[..., d // 2:])
            return jnp.concatenate([x1 * cos - x2 * sin, x2 * cos + x1 * sin], axis=-1)
        Bb, Tt, _ = x.shape
        cos, sin = _rope_tables(Tt, D_R)
        cos = cos[None]
        sin = sin[None]
        c_kv = x @ W_kv_down
        k_rope = _rotary_apply(c_kv @ W_k_rope, cos, sin)
        k = (c_kv @ W_k_up).reshape(Bb, Tt, NH, HD)
        v = (c_kv @ W_v_up).reshape(Bb, Tt, NH, HD)
        q = (x @ W_q).reshape(Bb, Tt, NH, HD)
        q_rope = _rotary_apply(x @ W_q_rope, cos, sin)
        scale = math.sqrt(HD + D_R)
        scores = jnp.einsum('bqhd,bkhd->bhqk', q, k)
        scores = scores + jnp.einsum('bqr,bkr->bqk', q_rope, k_rope)[:, None]
        scores = scores / scale
        causal = jnp.triu(jnp.ones((Tt, Tt), dtype=bool), k=1)
        scores = jnp.where(causal[None, None], -jnp.inf, scores)
        w = jax.nn.softmax(scores, axis=-1)
        attn = jnp.einsum('bhqk,bkhd->bqhd', w, v).reshape(Bb, Tt, D_MODEL)
        return attn @ W_o

    def _L0_attn_b_ref(x, qkv_weights):
        import jax, jax.numpy as jnp
        import numpy as np
        NUM_HEADS = 16
        USE_MASKING = True
        NEG_INF = -1000000000.0
        B, S, D = x.shape
        H = NUM_HEADS
        Dh = D // H
        qkv = jnp.einsum('bsd,de->bse', x, qkv_weights)
        qkv = qkv.reshape(-1, 3 * D)
        pre_q = qkv[:, 0 * D:1 * D].reshape(-1, S, H, Dh)
        pre_k = qkv[:, 1 * D:2 * D].reshape(-1, S, H, Dh)
        pre_v = qkv[:, 2 * D:3 * D].reshape(-1, S, H, Dh)
        q = jnp.transpose(pre_q, (0, 2, 1, 3)).reshape(-1, S, Dh)
        v = jnp.transpose(pre_v, (0, 2, 1, 3)).reshape(-1, S, Dh)
        k = jnp.transpose(pre_k, (0, 2, 3, 1)).reshape(-1, S, Dh)
        scale = jnp.asarray(np.sqrt(Dh), dtype=x.dtype)
        a = jnp.einsum('aib,ajb->aij', q, k) / scale
        if USE_MASKING:
            tril = jnp.tril(jnp.ones((S, S), dtype=x.dtype))[None]
            a = tril * a + NEG_INF * (1.0 - tril)
        a = jax.nn.softmax(a, axis=-1)
        heads = jnp.einsum('aij,ajb->aib', a, v)
        heads = heads.reshape(-1, H, S, Dh)
        heads = jnp.transpose(heads, (0, 2, 1, 3)).reshape(-1, S, D)
        return heads

    def _L0_ffn_ref(x, router_w, w1, b1, w2, b2):
        import jax, jax.numpy as jnp
        import numpy as np
        DIM = 128
        NUM_EXPERTS = 8
        HIDDEN = 512
        CAP_FACTOR = 2.0
        B, S = (4, 256)
        Bz, Sz, Dz = x.shape
        E = router_w.shape[0]
        capacity = max(1, int(Sz * CAP_FACTOR / E) + 1)
        scores = jax.nn.softmax(jnp.einsum('bsd,ed->bse', x, router_w), axis=-1)
        scores_t = jnp.swapaxes(scores, 1, 2)
        gate_vals, sel_idx = jax.lax.top_k(scores_t, capacity)
        b_idx = jnp.arange(Bz)[:, None, None]
        tokens = x[b_idx, sel_idx]
        h = jnp.einsum('becd,edh->bech', tokens, w1) + b1[None, :, None, :]
        h = jax.nn.gelu(h, approximate=False)
        y = jnp.einsum('bech,ehd->becd', h, w2) + b2[None, :, None, :]
        gated = y * gate_vals[..., None]
        out = jnp.zeros_like(x).at[b_idx, sel_idx].add(gated)
        return out
    x = L0_attn_a_x
    x = x + _L0_attn_a_ref(_layernorm(x, axis=-1), L0_attn_a_W_kv_down, L0_attn_a_W_k_up, L0_attn_a_W_v_up, L0_attn_a_W_q, L0_attn_a_W_q_rope, L0_attn_a_W_k_rope, L0_attn_a_W_o)
    x = x + _L0_ffn_ref(_layernorm(x, axis=-1), L0_ffn_router_w, L0_ffn_w1, L0_ffn_b1, L0_ffn_w2, L0_ffn_b2)
    x = x + _L0_attn_b_ref(_layernorm(x, axis=-1), L0_attn_b_qkv_weights)
    x = x + _L0_ffn_ref(_layernorm(x, axis=-1), L0_ffn_router_w, L0_ffn_w1, L0_ffn_b1, L0_ffn_w2, L0_ffn_b2)
    return x

_drawn_inputs = setup_inputs


def setup_inputs(seed=0):
    import zlib

    import numpy as np

    out = dict(_drawn_inputs(seed))
    spreads = {}
    factors = {'L0_ffn_b1': 4.541, 'L0_ffn_b2': 3.28}
    for name, (base, spread) in spreads.items():
        noise = np.random.default_rng([zlib.crc32(name.encode()), seed]).standard_normal(out[name].shape)
        drawn = base * np.exp(spread * noise) if base else spread * noise
        out[name] = jnp.asarray(drawn.astype(out[name].dtype))
    for name, factor in factors.items():
        out[name] = (out[name] * factor).astype(out[name].dtype)
    return out
```

```python
from contextlib import ExitStack

import concourse.bass as bass
import numpy as np
from concourse import mybir

ALU = mybir.AluOpType
ACT = mybir.ActivationFunctionType
AX = mybir.AxisListType
F32 = mybir.dt.float32
BF16 = mybir.dt.bfloat16
I32 = mybir.dt.int32
F32R = mybir.dt.float32r

P = 128
B, T, D = 2, 1024, 128
NT = B * T // P
NH, HD, DR = 16, 8, 32
CH = 512
NCH = B * T // CH
TPC = CH // P
NE, HID = 8, 512
HB = HID // P
CAPACITY = max(1, int(T * 2.0 / NE) + 1)
EPS = 1e-5

GH = 4
NG = NH // GH
GROUPS = B * NG
VW = 32
QSLOTS = {"a": (0, 0, 1, 1, 0, 2), "b": (0, 0, 1, 1, 0, 2, 1, 2, 2)}
KSLOTS = {"a": (0, 1, 0, 1, 2, 0), "b": (0, 1, 0, 1, 2, 0, 2, 1, 2)}
MSLOTS = {"a": 3, "b": 9}
NEG = -1.0e30

PAIRS = [(c, k) for c in range(T // CH) for k in range(0, TPC * (c + 1), 2)]
UNITS = len(PAIRS) * GH
PIECES = [[(0, 0, P, 0), (2, 0, 3 * P, P)], [(1, 0, 2 * P, 0), (5, CH, 2 * P, 2 * P)], [(3, 0, CH, 0)],
          [(4, 0, CH, 0)], [(4, CH, P, 0), (6, CH, 3 * P, P)], [(5, 0, CH, 0)], [(6, 0, CH, 0)],
          [(7, 0, CH, 0)], [(7, CH, CH, 0)]]
QT = T // P
HALF = UNITS // 2
GP = GH * len(PIECES)
SPLIT_STEPS = 6
SPLIT_STEPS = 6
UP = GP / UNITS


def unit_pieces(v):
    return [(x + GP // 2) % GP for x in range(int(v * UP), int((v + 1) * UP))]


def pair_tiles(pair):
    c, k0 = PAIRS[pair]
    out, col = [], 0
    for k in (k0, k0 + 1):
        first = max(0, k * P - c * CH)
        out.append((k, first, CH - first, col, k // TPC == c))
        col += CH - first
    return out, col


def chainer(engine, semaphore):
    count = [0]

    def link(instruction):
        count[0] += 1
        instruction.then_inc(semaphore, 1)
        engine.wait_ge(semaphore, count[0])

    return link


def first_signals(engine, semaphores):
    for semaphore in semaphores:
        engine.nop().then_inc(semaphore, 1)


def constants(nc, ctx, m, a):
    sem = lambda name: ctx.enter_context(nc.semaphore(name))
    zeroed, made, loaded, copied = sem("c_zeroed"), sem("c_made"), sem("c_loaded"), sem("c_copied")
    turned = sem("c_turned")
    with ExitStack() as local:
        sb = lambda name, shape, dt: local.enter_context(nc.sbuf_tensor(name, shape, dt))
        peers = sb("peers_f", [P, 2, P], F32)
        rw = sb("rw_rows", [NE, D], F32)
        b1 = sb("b1_rows", [NE * HB, P], F32)
        small = local.enter_context(nc.psum_tensor("c_turn", [P, CH], F32))
        with nc.Block() as block:

            @block.sync
            def _(sp):
                for c in range(NCH):
                    sp.dma_start(m.x[:, c * TPC:(c + 1) * TPC, :],
                                 a["x"].rearrange("b (t p) d -> p (b t) d", p=P)[:, c * TPC:(c + 1) * TPC, :]
                                 ).then_inc(loaded, 16)
                sp.dma_start(peers[:, :, :], a["peers"].rearrange("k p n -> p k n")).then_inc(loaded, 16)
                sp.dma_start(rw[:, :], a["router_w"]).then_inc(loaded, 16)
                sp.dma_start(b1[:, :], a["b1"].rearrange("e (j p) -> (e j) p", p=P)).then_inc(loaded, 16)
                sp.wait_ge(loaded, 16 * (NCH + 3))

            @block.gpsimd
            def _(pool):
                for t in (m.ident, m.ident_b, m.mask_st, m.mask_s):
                    pool.memset(t[:, :], 0.0).then_inc(zeroed, 1)
                pool.wait_ge(zeroed, 4)
                for t in (m.ident, m.ident_b):
                    pool.affine_select(out=t[:, :], in_=t[:, :], compare_op=ALU.not_equal, fill=1.0, base=0,
                                       pattern=[[-1, P]], channel_multiplier=1).then_inc(made, 1)
                pool.affine_select(out=m.mask_st[:, :], in_=m.mask_st[:, :], compare_op=ALU.is_ge, fill=NEG,
                                   base=0, pattern=[[1, P]], channel_multiplier=-1).then_inc(made, 1)
                pool.affine_select(out=m.mask_s[:, :], in_=m.mask_s[:, :], compare_op=ALU.is_ge, fill=NEG,
                                   base=0, pattern=[[-1, P]], channel_multiplier=1).then_inc(made, 1)

            @block.scalar
            def _(act):
                W = [(m.w_kv, a["W_kv_down"]), (m.w_k, a["W_k_up"]), (m.w_v, a["W_v_up"]), (m.w_q, a["W_q"]),
                     (m.w_o, a["W_o"]), (m.w_qkv, a["qkv"]), (m.tab, a["rope"].rearrange("k p t -> p k t")),
                     (m.tile_of, a["tile_of"])]
                for dst, src in W:
                    act.dma_start(dst[:], src).then_inc(m.weights_in, 16)
                for i, src in enumerate((a["W_q_rope"], a["W_k_rope"])):
                    act.dma_start(m.w_rope[:, i, 0, :], src).then_inc(m.weights_in, 16)
                    act.dma_start(m.w_rope[:, i, 1, :].rearrange("p (s r) -> p s r", s=2)[:, 0, :],
                                  src[:, DR // 2:DR]).then_inc(m.weights_in, 16)
                    act.dma_start(m.w_rope[:, i, 1, :].rearrange("p (s r) -> p s r", s=2)[:, 1, :],
                                  src[:, 0:DR // 2]).then_inc(m.weights_in, 16)
                act.dma_start(m.b2_rep[:, :], a["b2"].rearrange("(o e) d -> o e d", o=1).to_broadcast([NT, NE, D])
                              ).then_inc(m.weights_in, 16)
                act.wait_ge(m.weights_in, 16 * (len(W) + 6 + 1))

            @block.tensor
            def _(pe):
                pe.wait_ge(loaded, 16 * (NCH + 3))
                pe.wait_ge(made, 4)
                pe.transpose(small[:, 0:NE], rw[:, :], m.ident[0:NE, 0:NE]).then_inc(turned, 1)
                pe.transpose(small[:, P:P + NE * HB], b1[:, :], m.ident[0:NE * HB, 0:NE * HB]).then_inc(turned, 1)

            @block.vector
            def _(dve):
                dve.wait_ge(loaded, 16 * (NCH + 3))
                dve.tensor_copy(m.peers[:, :, :], peers[:, :, :]).then_inc(copied, 1)
                dve.wait_ge(turned, 2)
                dve.tensor_copy(m.rw_t[:, :], small[:, 0:NE]).then_inc(copied, 1)
                dve.tensor_copy(m.b1_t[:, :], small[:, P:P + NE * HB]).then_inc(copied, 1)


def norm_dve(nc, dve, m, s, st, mv, sc):
    for t in range(NT):
        dve.bn_stats(st[:, t, :], m.x[:, t, :]).then_inc(s.stats, 1)
    for t in range(NT):
        dve.wait_ge(s.stats, t + 1)
        dve.bn_aggr(mv[:, t, :], st[:, t, :]).then_inc(s.stats2, 1)
    dve.wait_ge(s.stats2, NT)
    link = chainer(dve, s.norm_chain)
    var, root, r, u = sc[:, 0, :], sc[:, 1, :], sc[:, 2, :], sc[:, 3, :]
    dve.tensor_scalar(var, mv[:, :, 1], EPS, None, ALU.add).then_inc(s.var_ready, 1)
    dve.wait_ge(s.root_ready, 1)
    link(dve.reciprocal(r, root))
    link(dve.tensor_tensor(u, r, r, ALU.mult))
    link(dve.tensor_tensor(u, u, var, ALU.mult))
    link(dve.tensor_scalar(u, u, -0.5, 1.5, ALU.mult, ALU.add))
    link(dve.tensor_tensor(r, r, u, ALU.mult))
    for t in range(NT):
        dve.tensor_scalar(m.xn[:, t, :], m.x[:, t, :], mv[:, t, 0:1], sc[:, 2, t:t + 1],
                          ALU.subtract, ALU.mult).then_inc(s.xn_ready, 1)


def norm_act_root(nc, act, s, sc):
    act.wait_ge(s.var_ready, 1)
    act.activation(sc[:, 1, :], sc[:, 0, :], ACT.Sqrt).then_inc(s.root_ready, 1)


class NormSemaphores:

    def __init__(self, sem):
        self.stats, self.stats2, self.norm_chain = sem("stats"), sem("stats2"), sem("norm_chain")
        self.var_ready, self.root_ready, self.xn_ready = sem("var_ready"), sem("root_ready"), sem("xn_ready")


class Memory:
    pass


def project(nc, ctx, m, a, kind):
    k = f"p{kind}"
    sem = lambda name: ctx.enter_context(nc.semaphore(f"{k}_{name}"))
    s = NormSemaphores(sem)
    turned, xt_ready, xt_free = sem("turned"), sem("xt_ready"), sem("xt_free")
    mm, ckv_ready, copied, split = sem("mm"), sem("ckv_ready"), sem("copied"), sem("split")
    chain, stored, first, ones_set = sem("chain"), sem("stored"), sem("first"), sem("ones_set")
    latent = kind == "a"
    with ExitStack() as local:
        sb = lambda name, shape, dt: local.enter_context(nc.sbuf_tensor(f"{k}_{name}", shape, dt))
        ps = lambda name, shape: local.enter_context(nc.psum_tensor(f"{k}_{name}", shape, F32))
        st, mv, sc = sb("st", [P, NT, 6], F32), sb("mv", [P, NT, 2], F32), sb("sc", [P, 4, NT], F32)
        xn_ps = ps("xn_ps", [P, 2, CH])
        one_ps, q_ps, k_ps, v_ps = ps("c_ps", [P, CH]), ps("q_ps", [P, CH]), ps("k_ps", [P, CH]), ps("v_ps", [P, CH])
        ckv = sb("ckv", [P, CH], F32)
        res = sb("res", [P, CH], F32)
        if latent:
            r_ps = ps("r_ps", [2 * DR, 2, CH])
            rot = sb("rot", [2 * DR, 2, CH], F32)
        parts = {"q": m.q_parts, "k": m.k_parts}
        n_mm = 5 if latent else 3

        def store(eng, name, b):
            for i in range(3):
                eng.dma_start(m.scratch[name][b * NG:(b + 1) * NG, i, :, :],
                              parts[name][:, i, b * T:(b + 1) * T]).then_inc(stored, 16)

        with nc.Block() as block:

            @block.vector
            def _(dve):
                norm_dve(nc, dve, m, s, st, mv, sc)
                link = chainer(dve, chain)

                def split_rest(src, dst, perm=None):
                    rows = src.shape[0]
                    shape = (lambda ap: ap.rearrange("p (s b) -> p b s", b=HD)) if perm else (lambda ap: ap)
                    left = res[0:rows, :].rearrange("p (b s) -> p b s", b=HD) if perm else res[0:rows, :]
                    link(dve.tensor_tensor(left, shape(src), dst[0], ALU.subtract))
                    link(dve.tensor_copy(dst[1], left))
                    link(dve.tensor_tensor(dst[2], left, dst[1], ALU.subtract))

                for c in range(NCH):
                    b, tok = c * CH // T, slice(c * CH, (c + 1) * CH)
                    dve.wait_ge(first, 2 * c + 1)
                    split_rest(q_ps[:, :], [m.q_parts[:, i, tok] for i in range(3)])
                    dve.wait_ge(first, 2 * c + 2)
                    split_rest(k_ps[:, :], [k_dst(m, kind, c, i) for i in range(3)], perm=not latent)
                    if latent:
                        dve.wait_ge(mm, n_mm * c + 4)
                        pos = slice(c * CH % T, c * CH % T + CH)
                        link(dve.tensor_tensor(rot[:, 0, :], r_ps[:, 0, :], m.tab[:, 0, pos], ALU.mult))
                        link(dve.tensor_tensor(rot[:, 1, :], r_ps[:, 1, :], m.tab[:, 1, pos], ALU.mult))
                        link(dve.tensor_tensor(rot[:, 0, :], rot[:, 0, :], rot[:, 1, :], ALU.add))
                        link(dve.tensor_copy(m.r_parts[:, 0, tok], rot[:, 0, :]))
                        split_rest(rot[:, 0, :], [m.r_parts[:, i, tok] for i in range(3)])
                    dve.nop().then_inc(split, 1)

            @block.scalar
            def _(act):
                norm_act_root(nc, act, s, sc)
                for c in range(NCH):
                    tok = slice(c * CH, (c + 1) * CH)
                    act.wait_ge(turned, c + 1)
                    act.activation(m.xt[:, tok], xn_ps[:, c % 2, :], ACT.Copy).then_inc(xt_ready, 1)
                    base = n_mm * c
                    if latent:
                        act.wait_ge(mm, base + 1)
                        act.activation(ckv[:, :], one_ps[:, :], ACT.Copy).then_inc(ckv_ready, 1)
                        base += 1
                    act.wait_ge(mm, base + 1)
                    act.activation(m.q_parts[:, 0, tok], q_ps[:, :], ACT.Copy).then_inc(first, 1)
                    act.wait_ge(mm, base + 2)
                    if latent:
                        act.activation(k_dst(m, kind, c, 0), k_ps[:, :], ACT.Copy).then_inc(first, 1)
                    else:
                        act.activation(k_dst(m, kind, c, 0), k_ps[:, :].rearrange("p (s b) -> p b s", b=HD),
                                       ACT.Copy).then_inc(first, 1)
                    act.wait_ge(mm, n_mm * (c + 1))
                    act.activation(m.v[:, c * TPC:(c + 1) * TPC, :],
                                   v_ps[:, :].rearrange("p (t n) -> p t n", t=TPC), ACT.Copy).then_inc(copied, 1)

            @block.tensor
            def _(pe):
                for c in range(NCH):
                    tok = slice(c * CH, (c + 1) * CH)
                    for i in range(TPC):
                        pe.wait_ge(s.xn_ready, c * TPC + i + 1)
                        if c >= 2 and i == 0:
                            pe.wait_ge(xt_ready, c - 1)
                        last = pe.transpose(xn_ps[:, c % 2, i * P:(i + 1) * P], m.xn[:, c * TPC + i, :], m.ident[:, :])
                    last.then_inc(turned, 1)
                    pe.wait_ge(xt_ready, c + 1)
                    xt = m.xt[:, tok]
                    if c:
                        pe.wait_ge(split, c)
                        pe.wait_ge(copied, c)
                    if latent:
                        pe.matmul(one_ps[:, :], m.w_kv[:, :], xt, start=True, stop=True).then_inc(mm, 1)
                        pe.matmul(q_ps[:, :], m.w_q[:, :], xt, start=True, stop=True).then_inc(mm, 1)
                        pe.wait_ge(ckv_ready, c + 1)
                        pe.matmul(k_ps[:, :], m.w_k[:, :], ckv[:, :], start=True, stop=True).then_inc(mm, 1)
                        for sw in range(2):
                            pe.matmul(r_ps[0:DR, sw, :], m.w_rope[:, 0, sw, :], xt, start=True, stop=True)
                            last = pe.matmul(r_ps[DR:2 * DR, sw, :], m.w_rope[:, 1, sw, :], ckv[:, :],
                                             start=True, stop=True)
                        last.then_inc(mm, 1)
                        for i in range(TPC):
                            last = pe.matmul(v_ps[:, i * P:(i + 1) * P], ckv[:, i * P:(i + 1) * P], m.w_v[:, :],
                                             start=True, stop=True)
                    else:
                        pe.matmul(q_ps[:, :], m.w_qkv[:, 0:D], xt, start=True, stop=True).then_inc(mm, 1)
                        pe.matmul(k_ps[:, :], m.w_qkv[:, D:2 * D], xt, start=True, stop=True).then_inc(mm, 1)
                        for i in range(TPC):
                            last = pe.matmul(v_ps[:, i * P:(i + 1) * P], m.xt[:, c * CH + i * P:c * CH + (i + 1) * P],
                                             m.w_qkv[:, 2 * D:3 * D], start=True, stop=True)
                    last.then_inc(mm, 1)

            @block.gpsimd
            def _(pool):
                link = chainer(pool, ones_set)
                first_row = (2 * DR if latent else 0) + len(QSLOTS[kind]) * HD
                q0 = first_row // 32 * 32
                for par in range(2):
                    link(pool.memset(m.k2[par][q0:q0 + 32, :, :], 1.0))
                if latent:
                    for par in range(2):
                        link(pool.memset(m.vg[par][:, :, :, :], 0.0))
                    for par in range(2):
                        link(pool.memset(m.vg[par][:, :, :, HD:HD + 1], 1.0))

            @block.sync
            def _(sp):
                for b in range(B):
                    sp.wait_ge(split, (b + 1) * T // CH)
                    store(sp, "q", b)
                    store(sp, "k", b)
                sp.wait_ge(stored, 16 * B * 2 * 3)


def k_dst(m, kind, c, part):
    if kind == "a":
        return m.k_parts[:, part, c * CH:(c + 1) * CH]
    b, s0, n = c * CH // T, (c * CH % T) // HD, CH // HD
    return m.k_parts[:, part, b * T:(b + 1) * T].rearrange("p (b s) -> p b s", b=HD)[:, :, s0:s0 + n]


def attention(nc, ctx, m, kind):
    k = f"t{kind}"
    latent = kind == "a"
    sem = lambda name: ctx.enter_context(nc.semaphore(f"{k}_{name}"))
    scale = float(1.0 / np.sqrt(HD + DR)) if latent else float(1.0 / np.sqrt(HD))
    QSLOT, KSLOT, MSLOT = QSLOTS[kind], KSLOTS[kind], MSLOTS[kind]
    NSLOT = len(QSLOT)
    R2 = 2 * DR if latent else 0
    RM = MSLOT * DR if latent else 0
    HR = NSLOT * HD
    M0 = R2 + HR
    K2, KM = M0 + 3, RM + MSLOT * HD
    n_loads2 = 2 * NSLOT + (2 * (2 + 4) if latent else 0)
    n_loadsm = 2 * MSLOT + (2 * MSLOT if latent else 0)

    op2_in, opm_in, m_in = [[sem(f"{n}{i}") for i in range(2)] for n in ("op2_in", "opm_in", "m_in")]
    v_ready = sem("v_ready")
    st_ready, exp_done, pv_done = sem("st_ready"), sem("exp_done"), sem("pv_done")
    mx_ready, mx_done = sem("mx_ready"), sem("mx_done")
    m_parts_ready, m_turned, m_copied, m_chain = sem("m_parts_ready"), sem("m_turned"), sem("m_copied"), sem("m_chain")
    o_copied, o_turned, o_done, o_chain = sem("o_copied"), sem("o_turned"), sem("o_done"), sem("o_chain")

    with ExitStack() as local:
        sb = lambda name, shape, dt: local.enter_context(nc.sbuf_tensor(f"{k}_{name}", shape, dt))
        ps = lambda name, shape, dt=F32: local.enter_context(nc.psum_tensor(f"{k}_{name}", shape, dt))
        q2 = [sb(f"q2_{i}", [P, GH, T], BF16) for i in range(2)]
        k2, vg = m.k2, m.vg
        qm = [sb(f"qm_{i}", [P, GH, T], BF16) for i in range(2)]
        km = [sb(f"km_{i}", [P, GH, T], BF16) for i in range(2)]
        if latent:
            qr = [sb(f"qr_{i}", [P, T], BF16) for i in range(2)]
            kr = [sb(f"kr_{i}", [P, T], BF16) for i in range(2)]
        pt = [sb(f"pt_{i}", [P, GH, 2 * CH], F32) for i in range(2)]
        mrow = [sb(f"mrow_{i}", [P, GH, QT + QT // 2], F32) for i in range(2)]
        mleft = sb("mleft", [P, GH, QT], F32)
        mparts = sb("mparts", [P, 3, GH, QT], BF16)
        mt = sb("mt", [3 * GH * T // P, P], BF16)
        ot = sb("ot", [P, CH], F32)
        rsum = sb("rsum", [P, TPC, GH], F32)
        st = [ps(f"st_{i}", [P, 2 * CH]) for i in range(2)]
        mx = ps("mx", [P, 2, CH])
        o_ps = ps("o_ps", [P, CH])
        t_ps = ps("t_ps", [P, CH])
        GT = GH * T // P

        def m_turn_ap():
            return t_ps[0:3 * GT, 0:P // 2].bitcast(BF16)

        unit = lambda n, v: 1 + n * UNITS + v
        pair = lambda n, p: 1 + n * len(PAIRS) + p
        piece = lambda n, v: 1 + n * GP + v
        chunk = lambda n, c: 1 + n * (T // CH) + c

        def loop(engine, body):
            with engine.Fori(0, GROUPS // 2 - 1) as i:
                for par in range(2):
                    body(i * 2 + par, par, True, True)
            body(GROUPS - 2, 0, True, False)
            body(GROUPS - 1, 1, False, False)

        with nc.Block() as block:

            @block.sync
            def _(sp):
                def load_m(n, par):
                    for side, t, slots in (("q", qm, QSLOT), ("k", km, KSLOT)):
                        for i in range(MSLOT):
                            sp.dma_start(t[par][RM + HD * i:RM + HD * (i + 1), :, :],
                                         head_rows(side, n, slots[i])).then_inc(opm_in[par], 16)

                def load_2(n, par):
                    for side, t, slots in (("q", q2, QSLOT), ("k", k2, KSLOT)):
                        for i in range(NSLOT):
                            sp.dma_start(t[par][R2 + HD * i:R2 + HD * (i + 1), :, :],
                                         head_rows(side, n, slots[i])).then_inc(op2_in[par], 16)

                def head_rows(side, n, part):
                    src = m.scratch[side][n, part, :, :]
                    if side == "q" or latent:
                        return src.rearrange("(h d) t -> d h t", d=HD)
                    return src.rearrange("(h d) (b s) -> b h d s", h=GH, b=HD)

                def rope_rows(par, b, which):
                    for side, r0 in (("q", 0), ("k", DR)):
                        slots = QSLOT if side == "q" else KSLOT
                        if which == "m":
                            t = qm if side == "q" else km
                            for i in range(MSLOT):
                                src = m.r_parts[r0:r0 + DR, slots[i], bass.ds(b * T, T)]
                                sp.dma_start(t[par][DR * i:DR * (i + 1), :, :],
                                             src.rearrange("p (o t) -> p o t", o=1).to_broadcast([DR, GH, T])
                                             ).then_inc(opm_in[par], 16)
                        else:
                            t, tr = (q2, qr) if side == "q" else (k2, kr)
                            for i in range(NSLOT):
                                src = m.r_parts[r0:r0 + DR, slots[i], bass.ds(b * T, T)]
                                if i < 4:
                                    sp.dma_start(tr[par][DR * i:DR * (i + 1), :], src).then_inc(op2_in[par], 16)
                                else:
                                    sp.dma_start(t[par][DR * (i - 4):DR * (i - 3), :, :],
                                                 src.rearrange("p (o t) -> p o t", o=1).to_broadcast([DR, GH, T])
                                                 ).then_inc(op2_in[par], 16)

                def m_rows(par):
                    for i in range(3):
                        sp.dma_start(q2[par][M0 + i:M0 + i + 1, :, :].rearrange("o h (q t) -> o (h q) t", t=P),
                                     mt[i * GT:(i + 1) * GT, :]).then_inc(m_in[par], 16)

                for n in range(2):
                    load_m(n, n)
                    if latent:
                        rope_rows(n, 0, "m")
                load_2(0, 0)
                if latent:
                    rope_rows(0, 0, "2")
                sp.wait_ge(m_copied, 1)
                m_rows(0)

                def body(n, par, ahead1, ahead2):
                    if ahead2:
                        sp.wait_ge(mx_ready, piece(n + 1, 0))
                        load_m(n + 2, par)
                        if latent:
                            rope_rows(par, batch_of(n + 2), "m")
                    if ahead1:
                        sp.wait_ge(st_ready, unit(n, 0))
                        load_2(n + 1, 1 - par)
                        if latent:
                            rope_rows(1 - par, batch_of(n + 1), "2")
                    if ahead1:
                        sp.wait_ge(m_copied, n + 2)
                        m_rows(1 - par)

                def batch_of(n):
                    return n // NG if isinstance(n, int) else n // NG

                loop(sp, body)

            @block.gpsimd
            def _(pool):
                def copy_v(n, par, b, g):
                    pool.tensor_copy(vg[par][:, :, :, 0:HD],
                                     m.v[:, bass.ds(b * (T // P), T // P), bass.ds(g * GH * HD, GH * HD)]
                                     .rearrange("p t (h d) -> p t h d", h=GH)).then_inc(v_ready, 1)

                copy_v(0, 0, 0, 0)

                def body(n, par, ahead1, ahead2):
                    if ahead1:
                        pool.wait_ge(pv_done, pair(n, 0))
                        copy_v(n + 1, 1 - par, (n + 1) // NG, (n + 1) % NG)

                loop(pool, body)

            @block.tensor
            def _(pe):
                def max_piece(n, par, v):
                    h, pc = divmod(v, len(PIECES))
                    if v == 0:
                        pe.wait_ge(opm_in[par], (n // 2 + 1) * 16 * n_loadsm)
                    if not (isinstance(n, int) and n == 0 and v < 2):
                        pe.wait_ge(mx_done, piece(n, v - 1))
                    for q, k0, w, col in PIECES[pc]:
                        diagonal = k0 + w == (q + 1) * P
                        last = pe.matmul(mx[:, v % 2, col:col + w], qm[par][0:KM, h, q * P:(q + 1) * P],
                                         km[par][0:KM, h, k0:k0 + w], start=True, stop=not diagonal,
                                         skip_group_check=True)
                        if diagonal:
                            last = pe.matmul(mx[:, v % 2, col + w - P:col + w], m.ident_b[:, :], m.mask_s[:, :],
                                             start=False, stop=True, skip_group_check=True)
                    last.then_inc(mx_ready, 1)

                def score_unit(n, par, v):
                    p, h = divmod(v, GH)
                    if v == 0:
                        pe.wait_ge(op2_in[par], (n // 2 + 1) * 16 * n_loads2)
                        pe.wait_ge(m_in[par], (n // 2 + 1) * 16 * 3)
                    if not (isinstance(n, int) and n == 0 and v < 2):
                        pe.wait_ge(exp_done, unit(n, v - 1))
                    for key, q0, w, col, diagonal in pair_tiles(p)[0]:
                        q = slice(PAIRS[p][0] * CH + q0, PAIRS[p][0] * CH + q0 + w)
                        out = st[v % 2][:, col:col + w]
                        if latent:
                            pe.matmul(out, kr[par][:, key * P:(key + 1) * P], qr[par][:, q],
                                      start=True, stop=False, skip_group_check=True)
                        last = pe.matmul(out, k2[par][0:K2, h, key * P:(key + 1) * P], q2[par][0:K2, h, q],
                                         start=not latent, stop=not diagonal, skip_group_check=True)
                        if diagonal:
                            last = pe.matmul(st[v % 2][:, col:col + P], m.ident_b[:, :], m.mask_st[:, :],
                                             start=False, stop=True, skip_group_check=True)
                    last.then_inc(st_ready, 1)

                def values(n, par, p):
                    pe.wait_ge(exp_done, unit(n, (p + 1) * GH))
                    if p == 0:
                        pe.wait_ge(v_ready, n + 1)
                    if PAIRS[p][1] == 0:
                        pe.wait_ge(o_copied, chunk(n, PAIRS[p][0]))
                    for key, q0, w, col, diagonal in pair_tiles(p)[0]:
                        for h in range(GH):
                            last = pe.matmul(o_ps[VW * h:VW * (h + 1), q0:CH], vg[par][:, key, h, :],
                                             pt[p % 2][:, h, col:col + w], start=(key == 0),
                                             stop=(key == TPC * (PAIRS[p][0] + 1) - 1), skip_group_check=True)
                    last.then_inc(pv_done, 1)

                def turn_out(n, c):
                    pe.wait_ge(o_copied, chunk(n, c + 1))
                    pe.wait_ge(o_done, chunk(n, c))
                    for i in range(TPC):
                        last = pe.transpose(t_ps[:, i * P:(i + 1) * P], ot[:, i * P:(i + 1) * P], m.ident[:, :])
                    last.then_inc(o_turned, 1)

                def turn_m(n):
                    pe.wait_ge(m_parts_ready, n + 1)
                    pe.transpose(m_turn_ap(), mparts[:, :, :, :].rearrange("p a h q -> p (a h q)"),
                                 m.ident_b[:, :]).then_inc(m_turned, 1)

                first_signals(pe, (st_ready, pv_done, mx_ready, o_turned))
                for v in range(GP):
                    max_piece(0, 0, v)
                turn_m(0)
                for v in range(GP // 2):
                    max_piece(1, 1, v)
                for v in range(2):
                    score_unit(0, 0, v)

                def body(n, par, ahead1, ahead2):
                    for p in range(len(PAIRS)):
                        for h in range(GH):
                            v = p * GH + h
                            if v >= 2:
                                score_unit(n, par, v)
                            for x in unit_pieces(v):
                                if v < HALF and ahead1:
                                    max_piece(n + 1, 1 - par, x)
                                if v >= HALF and ahead2:
                                    max_piece(n + 2, par, x)
                            if p and h == 1:
                                values(n, par, p - 1)
                            if p == 3 and h == 3:
                                pe.wait_ge(m_copied, n + 1)
                                turn_out(n, 0)
                            if p == 4 and h == 3 and ahead1:
                                pe.wait_ge(o_done, chunk(n, 1))
                                turn_m(n + 1)
                    if ahead1:
                        score_unit(n + 1, 1 - par, 0)
                    values(n, par, len(PAIRS) - 1)
                    if ahead1:
                        score_unit(n + 1, 1 - par, 1)
                        pe.wait_ge(m_copied, n + 2)
                    turn_out(n, 1)

                loop(pe, body)

            @block.scalar
            def _(act):
                def copy_o(n, p):
                    act.wait_ge(pv_done, pair(n, p + 1))
                    act.wait_ge(o_turned, chunk(n, PAIRS[p][0]))
                    act.activation(ot[:, :], o_ps[:, :], ACT.Copy).then_inc(o_copied, 1)

                def body(n, par, ahead1, ahead2):
                    for p in range(len(PAIRS)):
                        for h in range(GH):
                            v = p * GH + h
                            cols = pair_tiles(p)[1]
                            act.wait_ge(st_ready, unit(n, v + 1))
                            if h == 0:
                                act.wait_ge(pv_done, pair(n, max(p - 1, 0)))
                            act.activation(pt[p % 2][:, h, 0:cols], st[v % 2][:, 0:cols], ACT.Exp,
                                           scale=scale).then_inc(exp_done, 1)
                            if p == 2 and h == 2:
                                copy_o(n, 1)
                    copy_o(n, len(PAIRS) - 1)

                first_signals(act, (exp_done, o_copied))
                loop(act, body)

            @block.vector
            def _(dve):
                def take_max(n, par, v):
                    h, pc = divmod(v, len(PIECES))
                    dve.wait_ge(mx_ready, piece(n, v + 1))
                    for q, k0, w, col in PIECES[pc]:
                        at = q if k0 == 0 else q + QT // 2
                        last = dve.tensor_reduce(mrow[par][:, h, at:at + 1], mx[:, v % 2, col:col + w], AX.X,
                                                 ALU.max, negate=True)
                    last.then_inc(mx_done, 1)

                def split_m(n, par, step):
                    top, second = mrow[par][:, :, 0:QT], mrow[par][:, :, QT:]
                    if step == 0:
                        dve.wait_ge(mx_done, piece(n + 1, 0))
                        dve.tensor_tensor(mrow[par][:, :, QT // 2:QT], mrow[par][:, :, QT // 2:QT], second,
                                          ALU.min).then_inc(m_chain, 1)
                        return
                    dve.wait_ge(m_chain, n * (SPLIT_STEPS - 1) + step)
                    if step == 1:
                        dve.tensor_copy(mparts[:, 0, :, :], top).then_inc(m_chain, 1)
                    if step == 2:
                        dve.tensor_tensor(mleft[:, :, :], top, mparts[:, 0, :, :], ALU.subtract).then_inc(m_chain, 1)
                    if step == 3:
                        dve.tensor_copy(mparts[:, 1, :, :], mleft[:, :, :]).then_inc(m_chain, 1)
                    if step == 4:
                        dve.tensor_tensor(mleft[:, :, :], mleft[:, :, :], mparts[:, 1, :, :],
                                          ALU.subtract).then_inc(m_chain, 1)
                    if step == 5:
                        dve.tensor_copy(mparts[:, 2, :, :], mleft[:, :, :]).then_inc(m_parts_ready, 1)

                def copy_m(n, par):
                    dve.wait_ge(m_turned, n + 1)
                    if not (isinstance(n, int) and n == 0):
                        dve.wait_ge(m_in[1 - par], ((n - 1) // 2 + 1) * 16 * 3)
                    dve.tensor_copy(mt[:, :], m_turn_ap()).then_inc(m_copied, 1)

                def normalise(n, c, b, g):
                    dve.wait_ge(o_turned, chunk(n, c + 1))
                    turned = t_ps[:, :].rearrange("p (i h w) -> p i h w", i=TPC, h=GH)
                    dve.reciprocal(rsum[:, :, :], turned[:, :, :, HD]).then_inc(o_chain, 1)
                    dve.wait_ge(o_chain, n * 2 + c + 1)
                    dst = m.attn[:, bass.ds(b * QT + c * TPC, TPC), bass.ds(g * GH * HD, GH * HD)]
                    each = rsum[:, :, :].rearrange("p i (h o) -> p i h o", o=1).to_broadcast([P, TPC, GH, HD])
                    dve.tensor_tensor(dst.rearrange("p t (h d) -> p t h d", h=GH), turned[:, :, :, 0:HD], each,
                                      ALU.mult).then_inc(o_done, 1)

                first_signals(dve, (mx_done, o_done))
                for v in range(GP):
                    take_max(0, 0, v)
                for step in range(SPLIT_STEPS):
                    split_m(0, 0, step)
                copy_m(0, 0)
                for v in range(GP // 2):
                    take_max(1, 1, v)

                def body(n, par, ahead1, ahead2):
                    b, g = n // NG, n % NG
                    for p in range(len(PAIRS)):
                        for h in range(GH):
                            v = p * GH + h
                            for x in unit_pieces(v):
                                if v < HALF and ahead1:
                                    take_max(n + 1, 1 - par, x)
                                if v >= HALF and ahead2:
                                    take_max(n + 2, par, x)
                            if HALF <= v < HALF + SPLIT_STEPS and ahead1:
                                split_m(n + 1, 1 - par, v - HALF)
                            if p == 4 and h == 0:
                                normalise(n, 0, b, g)
                            if p == 5 and h == 0 and ahead1:
                                copy_m(n + 1, 1 - par)
                    normalise(n, 1, b, g)

                loop(dve, body)


def output_projection(nc, ctx, m):
    sem = lambda name: ctx.enter_context(nc.semaphore(f"o_{name}"))
    turned, copied, mm, added = sem("turned"), sem("copied"), sem("mm"), sem("added")
    with ExitStack() as local:
        t_ps = local.enter_context(nc.psum_tensor("o_t", [P, 2, CH], F32))
        y_ps = local.enter_context(nc.psum_tensor("o_y", [P, 2, CH], F32))
        with nc.Block() as block:

            @block.tensor
            def _(pe):
                for c in range(NCH):
                    if c >= 2:
                        pe.wait_ge(copied, c - 1)
                    for i in range(TPC):
                        last = pe.transpose(t_ps[:, c % 2, i * P:(i + 1) * P], m.attn[:, c * TPC + i, :], m.ident[:, :])
                    last.then_inc(turned, 1)
                    pe.wait_ge(copied, c + 1)
                    if c >= 2:
                        pe.wait_ge(added, c - 1)
                    for i in range(TPC):
                        last = pe.matmul(y_ps[:, c % 2, i * P:(i + 1) * P],
                                         m.xt[:, c * CH + i * P:c * CH + (i + 1) * P], m.w_o[:, :],
                                         start=True, stop=True)
                    last.then_inc(mm, 1)

            @block.scalar
            def _(act):
                for c in range(NCH):
                    act.wait_ge(turned, c + 1)
                    act.activation(m.xt[:, c * CH:(c + 1) * CH], t_ps[:, c % 2, :], ACT.Copy).then_inc(copied, 1)

            @block.vector
            def _(dve):
                for c in range(NCH):
                    dve.wait_ge(mm, c + 1)
                    xc = m.x[:, c * TPC:(c + 1) * TPC, :].rearrange("p t n -> p (t n)")
                    dve.tensor_tensor(xc, xc, y_ps[:, c % 2, :], ALU.add).then_inc(added, 1)


def add_heads(nc, ctx, m):
    added = ctx.enter_context(nc.semaphore("h_added"))
    with nc.Block() as block:

        @block.vector
        def _(dve):
            for c in range(NCH):
                xc, hc = (t[:, c * TPC:(c + 1) * TPC, :] for t in (m.x, m.attn))
                dve.tensor_tensor(xc, xc, hc, ALU.add).then_inc(added, 1)


def route(nc, ctx, m, a, k):
    sem = lambda name: ctx.enter_context(nc.semaphore(f"r{k}_{name}"))
    s = NormSemaphores(sem)
    turned, xt_ready, logits_ready = sem("turned"), sem("xt_ready"), sem("logits_ready")
    chain, shifted, exp_done, score_ready, t_turned = sem("chain"), sem("shifted"), sem("exp_done"), sem("score_ready"), sem("t_turned")
    count_ready, total_ready, gate_ready, g_turned, gate_copied = sem("count_ready"), sem("total_ready"), sem("gate_ready"), sem("g_turned"), sem("gate_copied")
    bias_rows, bias_mm, bias_added = sem("bias_rows"), sem("bias_mm"), sem("bias_added")
    BITS = range(29, -1, -1)
    with ExitStack() as local:
        sb = lambda name, shape, dt=F32: local.enter_context(nc.sbuf_tensor(f"r{k}_{name}", shape, dt))
        ps = lambda name, shape: local.enter_context(nc.psum_tensor(f"r{k}_{name}", shape, F32))
        st, mv, sc = sb("st", [P, NT, 6]), sb("mv", [P, NT, 2]), sb("sc", [P, 4, NT])
        xn_ps, l_ps, t_ps, c_ps = ps("xn_ps", [P, 2, CH]), ps("l_ps", [P, NT * NE]), ps("t_ps", [P, CH]), ps("c_ps", [P, 8])
        b_ps = ps("b_ps", [P, 2, CH])
        peak, e, total, score = sb("peak", [P, NT]), sb("e", [P, NT, NE]), sb("total", [P, NT]), sb("score", [P, NT, NE])
        rows = sb("rows", [P, P])
        trial = sb("trial", [P, 1], I32)
        drop = sb("drop", [P, 1], I32)
        above, count, totals = sb("above", [P, P]), sb("count", [P, 2], BF16), sb("totals", [P, 2])
        tied, order, need, take = sb("tied", [P, P]), sb("order", [P, P]), sb("need", [P, 1]), sb("take", [P, P])
        gate_rows = sb("gate_rows", [P, P])
        b2_sel = sb("b2_sel", [P, 4, D])
        n_count = len(BITS) + 1

        with nc.Block() as block:

            @block.vector
            def _(dve):
                norm_dve(nc, dve, m, s, st, mv, sc)
                link = chainer(dve, chain)
                for r in range(4):
                    link(dve.tensor_scalar(b2_sel[:, r, :], m.b2_rep[:, :], m.tile_of[:, r:r + 1], None, ALU.mult))
                dve.memset(trial[:, :], 1 << BITS[0]).then_inc(bias_rows, 1)
                dve.wait_ge(logits_ready, 1)
                l = l_ps[:, :].rearrange("p (t e) -> p t e", e=NE)
                each = lambda ap: ap.rearrange("p (t o) -> p t o", o=1).to_broadcast([P, NT, NE])
                link(dve.tensor_reduce(peak[:, :], l, AX.X, ALU.max))
                dve.tensor_tensor(e[:, :, :], l, each(peak[:, :]), ALU.subtract).then_inc(shifted, 1)
                dve.wait_ge(exp_done, 1)
                link(dve.tensor_reduce(total[:, :], e[:, :, :], AX.X, ALU.add))
                link(dve.reciprocal(total[:, :], total[:, :]))
                dve.tensor_tensor(score[:, :, :], e[:, :, :], each(total[:, :]), ALU.mult).then_inc(score_ready, 1)
                dve.wait_ge(t_turned, 1)
                link(dve.tensor_copy(rows[:, :], t_ps[:, 0:P]))
                dve.wait_ge(bias_rows, 1)
                for i, bit in enumerate(BITS):
                    dve.tensor_scalar(above[:, :], rows[:, :], trial[:, :].bitcast(F32), 0.0, ALU.is_ge,
                                      ALU.add, accum_out=count[:, 0:1]).then_inc(count_ready, 1)
                    dve.wait_ge(total_ready, i + 1)
                    link(dve.tensor_scalar(drop[:, :], c_ps[:, 0:1], CAPACITY - 0.5, float(1 << bit), ALU.is_lt,
                                           ALU.mult))
                    link(dve.scalar_tensor_tensor(out=trial[:, :], in0=drop[:, :], scalar=(1 << bit) >> 1,
                                                  in1=trial[:, :], op0=ALU.bitwise_or, op1=ALU.bitwise_xor))
                limit = trial[:, :].bitcast(F32)
                link(dve.tensor_scalar(above[:, :], rows[:, :], limit, 0.0, ALU.is_gt, ALU.add,
                                       accum_out=count[:, 0:1]))
                dve.tensor_scalar(tied[:, :], rows[:, :], limit, 0.0, ALU.is_equal, ALU.add,
                                  accum_out=count[:, 1:2]).then_inc(count_ready, 1)
                dve.wait_ge(count_ready, n_count)
                link(dve.tensor_tensor_scan(order[:, :], m.ones[:, :], tied[:, :], 0.0, ALU.mult, ALU.add))
                dve.wait_ge(total_ready, n_count)
                link(dve.tensor_copy(totals[:, :], c_ps[:, 0:2]))
                link(dve.tensor_tensor(need[:, :], totals[:, 0:1], totals[:, 1:2], ALU.add))
                link(dve.tensor_scalar(need[:, :], need[:, :], -1.0, float(CAPACITY), ALU.mult, ALU.add))
                link(dve.tensor_scalar(order[:, :], order[:, :], need[:, 0:1], None, ALU.is_le))
                link(dve.tensor_tensor(tied[:, :], tied[:, :], order[:, :], ALU.mult))
                link(dve.tensor_tensor(take[:, :], above[:, :], tied[:, :], ALU.add))
                dve.tensor_tensor(gate_rows[:, :], rows[:, :], take[:, :], ALU.mult).then_inc(gate_ready, 1)
                dve.wait_ge(g_turned, 1)
                dve.tensor_copy(m.gate[:, :], t_ps[:, P:2 * P]).then_inc(gate_copied, 1)
                for c in range(NCH):
                    dve.wait_ge(bias_mm, c + 1)
                    xc = m.x[:, c * TPC:(c + 1) * TPC, :].rearrange("p t n -> p (t n)")
                    dve.tensor_tensor(xc, xc, b_ps[:, c % 2, :], ALU.add).then_inc(bias_added, 1)

            @block.scalar
            def _(act):
                norm_act_root(nc, act, s, sc)
                for c in range(NCH):
                    act.wait_ge(turned, c + 1)
                    act.activation(m.xt[:, c * CH:(c + 1) * CH], xn_ps[:, c % 2, :], ACT.Copy).then_inc(xt_ready, 1)
                act.wait_ge(shifted, 1)
                act.activation(e[:, :, :], e[:, :, :], ACT.Exp).then_inc(exp_done, 1)

            @block.tensor
            def _(pe):
                for c in range(NCH):
                    if c >= 2:
                        pe.wait_ge(xt_ready, c - 1)
                    for i in range(TPC):
                        pe.wait_ge(s.xn_ready, c * TPC + i + 1)
                        last = pe.transpose(xn_ps[:, c % 2, i * P:(i + 1) * P], m.xn[:, c * TPC + i, :], m.ident[:, :])
                    last.then_inc(turned, 1)
                for t in range(NT):
                    pe.wait_ge(xt_ready, t // TPC + 1)
                    last = pe.matmul(l_ps[:, t * NE:(t + 1) * NE], m.xt[:, t * P:(t + 1) * P], m.rw_t[:, :],
                                     start=True, stop=True)
                last.then_inc(logits_ready, 1)
                pe.wait_ge(score_ready, 1)
                pe.transpose(t_ps[:, 0:P], score[:, :, :].rearrange("p t e -> p (t e)"), m.ident[:, :]).then_inc(t_turned, 1)
                for i in range(len(BITS)):
                    pe.wait_ge(count_ready, i + 1)
                    pe.matmul(c_ps[:, 0:1], m.peers[:, 0, :], count[:, 0:1], start=True, stop=True).then_inc(total_ready, 1)
                pe.wait_ge(count_ready, n_count)
                pe.matmul(c_ps[:, 0:1], m.peers[:, 0, :], count[:, 0:1], start=True, stop=True)
                pe.matmul(c_ps[:, 1:2], m.peers[:, 1, :], count[:, 1:2], start=True, stop=True).then_inc(total_ready, 1)
                pe.wait_ge(gate_ready, 1)
                pe.transpose(t_ps[:, P:2 * P], gate_rows[:, :], m.ident[:, :]).then_inc(g_turned, 1)
                for c in range(NCH):
                    if c >= 2:
                        pe.wait_ge(bias_added, c - 1)
                    for i in range(TPC):
                        q = slice(32 * c, 32 * (c + 1))
                        last = pe.matmul(b_ps[:, c % 2, i * P:(i + 1) * P], gate_rows[q, :], b2_sel[q, i, :],
                                         start=True, stop=True)
                    last.then_inc(bias_mm, 1)


def experts(nc, ctx, m, a, k):
    sem = lambda name: ctx.enter_context(nc.semaphore(f"e{k}_{name}"))
    w_in = [sem(f"w_in{i}") for i in range(2)]
    x_high, x_split, w_high, w_split = sem("x_high"), sem("x_split"), sem("w_high"), sem("w_split")
    b1_set = sem("b1_set")
    h_mm, gelu_done, y_mm, added = sem("h_mm"), sem("gelu_done"), sem("y_mm"), sem("added")
    with ExitStack() as local:
        sb = lambda name, shape, dt=F32: local.enter_context(nc.sbuf_tensor(f"e{k}_{name}", shape, dt))
        ps = lambda name, shape: local.enter_context(nc.psum_tensor(f"e{k}_{name}", shape, F32))
        xr = [sb(f"xr_{i}", [P, B * T], F32R) for i in range(2)]
        w1r = [[sb(f"w1r_{i}_{j}", [P, HID], F32R) for j in range(2)] for i in range(2)]
        w1 = [sb(f"w1_{i}", [P, HID]) for i in range(2)]
        w2 = [sb(f"w2_{i}", [P, HB, D]) for i in range(2)]
        h = [sb(f"h_{i}", [P, HB, CH]) for i in range(2)]
        b1 = [sb(f"b1_{i}", [P, HB]) for i in range(2)]
        h_ps = ps("h_ps", [P, HB, CH])
        y_ps = ps("y_ps", [P, 2, CH])

        chunks = lambda e, c: 1 + e * NCH + c
        blocks = lambda e, c, j: 1 + e * (NCH * HB) + c * HB + j

        def loop(engine, body, signals):
            first_signals(engine, signals)
            with engine.Fori(0, NE // 2) as i:
                for par in range(2):
                    body(i * 2 + par, par)

        with nc.Block() as block:

            @block.sync
            def _(sp):
                def load(e, par):
                    sp.dma_start(w1[par][:, :], a["w1"][e, :, :]).then_inc(w_in[par], 16)
                    sp.dma_start(w2[par][:, :, :], a["w2"][e, :, :].rearrange("(j p) d -> p j d", p=P)).then_inc(w_in[par], 16)

                load(0, 0)
                load(1, 1)
                with sp.Fori(0, NE // 2 - 1) as i:
                    for par in range(2):
                        sp.wait_ge(y_mm, chunks(i * 2 + par + 1, 0))
                        sp.wait_ge(w_split, i * 2 + par + 1)
                        load(i * 2 + par + 2, par)

            @block.tensor
            def _(pe):
                def body(e, par):
                    def y(c):
                        pe.wait_ge(added, chunks(e, max(c - 1, 0)))
                        for i in range(TPC):
                            for j in range(HB):
                                if i == 0:
                                    pe.wait_ge(gelu_done, blocks(e, c, j + 1))
                                last = pe.matmul(y_ps[:, c % 2, i * P:(i + 1) * P], h[c % 2][:, j, i * P:(i + 1) * P],
                                                 w2[par][:, j, :], start=(j == 0), stop=(j == HB - 1))
                        last.then_inc(y_mm, 1)

                    pe.wait_ge(w_in[par], (e // 2 + 1) * 32)
                    pe.wait_ge(w_split, e + 1)
                    for c in range(NCH):
                        for j in range(HB):
                            pe.wait_ge(gelu_done, blocks(e, c - 1, j + 1) if c else blocks(e, 0, 0))
                            for i, (wp, xp) in enumerate(((0, 0), (0, 1), (1, 0))):
                                last = pe.matmul(h_ps[:, j, :], w1r[par][wp][:, j * P:(j + 1) * P],
                                                 xr[xp][:, c * CH:(c + 1) * CH], start=(i == 0), stop=(i == 2))
                            last.then_inc(h_mm, 1)
                        if c:
                            y(c - 1)
                    y(NCH - 1)

                pe.wait_ge(x_split, NCH)
                loop(pe, body, (h_mm, y_mm))

            @block.scalar
            def _(act):
                def body(e, par):
                    act.activation(b1[par][:, :], m.b1_t[:, bass.ds(e * HB, HB)], ACT.Copy).then_inc(b1_set, 1)
                    act.wait_ge(b1_set, e + 1)
                    for c in range(NCH):
                        act.wait_ge(y_mm, chunks(e, max(c - 1, 0)))
                        for j in range(HB):
                            act.wait_ge(h_mm, blocks(e, c, j + 1))
                            act.activation(h[c % 2][:, j, :], h_ps[:, j, :], ACT.Gelu,
                                           bias=b1[par][:, j:j + 1]).then_inc(gelu_done, 1)

                loop(act, body, (gelu_done,))

            @block.vector
            def _(dve):
                def split_w1(e, par):
                    dve.wait_ge(w_in[par], (e // 2 + 1) * 32)
                    dve.tensor_copy(w1r[par][0][:, :], w1[par][:, :]).then_inc(w_high, 1)
                    dve.wait_ge(w_high, e + 1)
                    dve.tensor_tensor(w1r[par][1][:, :], w1[par][:, :], w1r[par][0][:, :].bitcast(F32),
                                      ALU.subtract).then_inc(w_split, 1)

                for c in range(NCH):
                    dve.tensor_copy(xr[0][:, c * CH:(c + 1) * CH], m.xt[:, c * CH:(c + 1) * CH]).then_inc(x_high, 1)
                for c in range(NCH):
                    tok = slice(c * CH, (c + 1) * CH)
                    dve.wait_ge(x_high, c + 1)
                    dve.tensor_tensor(xr[1][:, tok], m.xt[:, tok], xr[0][:, tok].bitcast(F32),
                                      ALU.subtract).then_inc(x_split, 1)
                for e in range(2):
                    split_w1(e, e)

                def body(e, par):
                    for c in range(NCH):
                        dve.wait_ge(y_mm, chunks(e, c + 1))
                        dve.wait_ge(added, chunks(e, 0))
                        for i in range(TPC):
                            t = c * TPC + i
                            last = dve.scalar_tensor_tensor(out=m.x[:, t, :], in0=y_ps[:, c % 2, i * P:(i + 1) * P],
                                                            scalar=m.gate[:, bass.ds(e + t * NE, 1)], in1=m.x[:, t, :],
                                                            op0=ALU.mult, op1=ALU.add)
                        last.then_inc(added, 1)

                first_signals(dve, (added,))
                with dve.Fori(0, NE // 2 - 1) as i:
                    for par in range(2):
                        body(i * 2 + par, par)
                        split_w1(i * 2 + par + 2, par)
                for e in range(NE - 2, NE):
                    body(e, e % 2)


def block_kernel(nc, a, out):
    with ExitStack() as ctx:
        sb = lambda name, shape, dt=F32: ctx.enter_context(nc.sbuf_tensor(name, shape, dt))
        m = Memory()
        m.x = sb("x", [P, NT, D])
        m.xn = sb("xn", [P, NT, D])
        m.xt = sb("xt", [P, B * T])
        m.attn = sb("attn", [P, NT, D])
        m.v = sb("v", [P, NT, D])
        m.ident = sb("ident", [P, P])
        m.ident_b = sb("ident_b", [P, P], BF16)
        m.ones = sb("ones", [P, P])
        m.mask_st = sb("mask_st", [P, P], BF16)
        m.mask_s = sb("mask_s", [P, P], BF16)
        m.w_kv = sb("w_kv", [P, D])
        m.w_k = sb("w_k", [P, D])
        m.w_v = sb("w_v", [P, D])
        m.w_q = sb("w_q", [P, D])
        m.w_o = sb("w_o", [P, D])
        m.w_qkv = sb("w_qkv", [P, 3 * D])
        m.w_rope = sb("w_rope", [P, 2, 2, DR])
        m.tab = sb("tab", [2 * DR, 2, T])
        m.tile_of = sb("tile_of", [P, 4])
        m.b2_rep = sb("b2_rep", [P, D])
        m.peers = sb("peers", [P, 2, P], BF16)
        m.rw_t = sb("rw_t", [P, NE])
        m.b1_t = sb("b1_t", [P, NE * HB])
        m.gate = sb("gate", [P, NT * NE])
        m.k2 = [sb(f"k2_{i}", [P, GH, T], BF16) for i in range(2)]
        m.vg = [sb(f"vg_{i}", [P, T // P, GH, VW]) for i in range(2)]
        m.weights_in = ctx.enter_context(nc.semaphore("weights_in"))
        m.scratch = {n: nc.dram_tensor(f"scratch_{n}", (GROUPS, 3, GH * HD, T), BF16).ap() for n in "qk"}
        constants(nc, ctx, m, a)
        ones_set = ctx.enter_context(nc.semaphore("ones_set"))
        with nc.Block() as block:

            @block.vector
            def _(dve):
                dve.memset(m.ones[:, :], 1.0).then_inc(ones_set, 1)

        for k, kind in enumerate("ab"):
            with ExitStack() as local:
                part = lambda name, rows: local.enter_context(nc.sbuf_tensor(f"{name}_{kind}", [rows, 3, B * T], BF16))
                m.r_parts = part("r_parts", 2 * DR) if kind == "a" else None
                with ExitStack() as inner:
                    m.q_parts, m.k_parts = [inner.enter_context(nc.sbuf_tensor(f"{n}_parts_{kind}", [P, 3, B * T], BF16))
                                            for n in "qk"]
                    project(nc, ctx, m, a, kind)
                attention(nc, ctx, m, kind)
            if kind == "a":
                output_projection(nc, ctx, m)
            else:
                add_heads(nc, ctx, m)
            route(nc, ctx, m, a, k)
            experts(nc, ctx, m, a, k)

        stored = ctx.enter_context(nc.semaphore("out_stored"))
        with nc.Block() as block:

            @block.sync
            def _(sp):
                sp.dma_start(out.rearrange("b (t p) d -> p (b t) d", p=P), m.x[:, :, :]).then_inc(stored, 16)
                sp.wait_ge(stored, 16)


def tables():
    inv = (1.0 / np.float32(10000.0) ** (np.arange(0, DR, 2, dtype=np.float32) / np.float32(DR))).astype(np.float32)
    angle = np.outer(np.arange(T, dtype=np.float32), inv).astype(np.float32).T
    cos, sin = np.cos(angle), np.sin(angle)
    half = np.stack([np.concatenate([cos, cos]), np.concatenate([-sin, sin])])
    rope = np.concatenate([half, half], axis=1).astype(np.float32)
    p = np.arange(P)
    batch, tile, expert = p // (P // B), p // NE, p % NE
    same = (expert[:, None] == expert[None, :]) & (batch[:, None] == batch[None, :])
    peers = np.stack([same, same & (tile[:, None] < tile[None, :])]).astype(np.float32)
    tile_of = (tile[:, None] % 4 == np.arange(4)[None, :]).astype(np.float32)
    return {"rope": rope, "peers": peers, "tile_of": tile_of}


_INS = {"x": "L0_attn_a_x", "W_kv_down": "L0_attn_a_W_kv_down", "W_k_up": "L0_attn_a_W_k_up",
        "W_v_up": "L0_attn_a_W_v_up", "W_q": "L0_attn_a_W_q", "W_q_rope": "L0_attn_a_W_q_rope",
        "W_k_rope": "L0_attn_a_W_k_rope", "W_o": "L0_attn_a_W_o", "qkv": "L0_attn_b_qkv_weights",
        "router_w": "L0_ffn_router_w", "w1": "L0_ffn_w1", "b1": "L0_ffn_b1", "w2": "L0_ffn_w2", "b2": "L0_ffn_b2"}


def kernel(**inputs):
    import concourse.bacc as bacc
    from concourse.bass_utils import run_bass_kernel_spmd as run

    nc = bacc.Bacc("TRN2", target_bir_lowering=False, num_devices=1)
    arrays, args = {}, {}
    given = {short: np.ascontiguousarray(inputs[name]) for short, name in _INS.items()}
    for short, array in {**given, **tables()}.items():
        arrays[f"in_{short}"] = array
        args[short] = nc.dram_tensor(f"in_{short}", array.shape, mybir.dt.from_np(array.dtype),
                                              kind="ExternalInput").ap()
    out = nc.dram_tensor("out_0", (B, T, D), F32, kind="ExternalOutput").ap()
    block_kernel(nc, args, out)
    result = run(nc, [arrays], core_ids=[0])
    return result.results[0]["out_0"]
```
